# Optimizing a Trainium2 kernel written in Bass

```python
import numpy as np
import jax
import jax.numpy as jnp

def _softmax(x, axis=-1):
    return jax.nn.softmax(x, axis=axis)

def _gelu(x):
    return jax.nn.gelu(x, approximate=True)

def _silu(x):
    return jax.nn.silu(x)

def _sigmoid(x):
    return jax.nn.sigmoid(x)

def _layernorm(x, axis=-1, eps=1e-05):
    m = jnp.mean(x, axis=axis, keepdims=True)
    v = jnp.var(x, axis=axis, keepdims=True)
    return (x - m) / jnp.sqrt(v + eps)

def _scatter_add(tgt, idx, src, axis=0):
    return tgt.at[idx].add(src)

def _segment_sum(src, seg, n):
    return jax.ops.segment_sum(src, seg, n)
kernel_name = 'mk_adaln_ffn_d1_seqx_r2_ac289b'

def setup_inputs(seed: int=0):
    np.random.seed(seed)
    _w = jnp.asarray

    def _rec_inputs():
        import jax
        import jax.numpy as jnp
        _rk = jax.random.key(seed)
        x = -1.394e-06 + 0.9999 * jax.random.normal(jax.random.fold_in(_rk, 1), (4, 1024, 1024), jnp.float32)
        _lenS = 1024 - jax.random.randint(jax.random.fold_in(_rk, 7), (4,), 0, max(1, 1024 // 4) + 1, jnp.int32)
        _lenS2 = 1024 - jax.random.randint(jax.random.fold_in(_rk, 8), (4,), 0, max(1, 1024 // 4) + 1, jnp.int32)
        cond_2048 = -0.00499425 + 1.0058 * jax.random.normal(jax.random.fold_in(_rk, 11), (4, 1024), jnp.float32)
        return (x, cond_2048)
    x, cond_2048 = _rec_inputs()

    def _L0_cond_setup():
        import jax, jax.numpy as jnp
        import numpy as np
        B, T, D = (16, 128, 1024)
        key = jax.random.key(seed)
        k0, k1, k2, k3 = jax.random.split(key, 4)
        scale = 1.0 / np.sqrt(D)
        return {'initial_state': jax.random.normal(k0, (B, D), jnp.float32), 'inputs': jax.random.normal(k1, (B, T, D), jnp.float32), 'W_ih': jax.random.normal(k2, (D, 3 * D), jnp.float32) * scale, 'W_hh': jax.random.normal(k3, (D, 3 * D), jnp.float32) * scale, 'b_ih': jnp.zeros((3 * D,), jnp.float32), 'b_hh': jnp.zeros((3 * D,), jnp.float32)}
    _L0_cond_all = _L0_cond_setup()
    _L0_cond_in = {k: v for k, v in _L0_cond_all.items() if k in ('W_ih', 'W_hh', 'b_ih', 'b_hh')}
    del _L0_cond_all

    def _L0_ffn_setup():
        import jax, jax.numpy as jnp
        import numpy as np
        IN_F, OUT_F = (1024, 1024)
        N_EXPERTS, RANK, TOP_K = (8, 128, 2)
        key = jax.random.key(seed)
        k_x, k_r, k_a, k_b = jax.random.split(key, 4)
        hidden_states = jax.random.normal(k_x, (4, 2048, IN_F), dtype=jnp.float32)
        router_w = jax.random.normal(k_r, (IN_F, N_EXPERTS), dtype=jnp.float32) * IN_F ** (-0.5)
        Wa = jax.random.normal(k_a, (N_EXPERTS, IN_F, RANK), dtype=jnp.float32) * IN_F ** (-0.5)
        Wb = jax.random.normal(k_b, (N_EXPERTS, RANK, OUT_F), dtype=jnp.float32) * RANK ** (-0.5)
        return {'hidden_states': hidden_states, 'router_w': router_w, 'Wa': Wa, 'Wb': Wb}
    _L0_ffn_all = _L0_ffn_setup()
    _L0_ffn_in = {k: v for k, v in _L0_ffn_all.items() if k in ('router_w', 'Wa', 'Wb')}
    del _L0_ffn_all
    return {'x': x, 'cond_2048': cond_2048, 'L0_cond_W_ih': _L0_cond_in['W_ih'], 'L0_cond_W_hh': _L0_cond_in['W_hh'], 'L0_cond_b_ih': _L0_cond_in['b_ih'], 'L0_cond_b_hh': _L0_cond_in['b_hh'], 'L0_ffn_router_w': _L0_ffn_in['router_w'], 'L0_ffn_Wa': _L0_ffn_in['Wa'], 'L0_ffn_Wb': _L0_ffn_in['Wb']}

def reference(x, cond_2048, L0_cond_W_ih, L0_cond_W_hh, L0_cond_b_ih, L0_cond_b_hh, L0_ffn_router_w, L0_ffn_Wa, L0_ffn_Wb):
    import jax
    import jax.numpy as jnp

    def _L0_cond_ref(initial_state, inputs, W_ih, W_hh, b_ih, b_hh):
        import jax, jax.numpy as jnp
        import numpy as np
        B, T, D = (16, 128, 1024)
        "ScanOverTime(GRU cell): sequential per-timestep module call with\n            dict-state passing; merge_dict_trees stacks the per-step\n            'state_predicted' tensors along axis=1 -> [B, T, D]."

        def cell(h, x):
            gi = x @ W_ih + b_ih
            gh = h @ W_hh + b_hh
            i_r, i_z, i_n = jnp.split(gi, 3, axis=-1)
            h_r, h_z, h_n = jnp.split(gh, 3, axis=-1)
            r = jax.nn.sigmoid(i_r + h_r)
            z = jax.nn.sigmoid(i_z + h_z)
            n = jnp.tanh(i_n + r * h_n)
            h_new = (1.0 - z) * n + z * h
            return (h_new, h_new)
        xs = jnp.swapaxes(inputs, 0, 1)
        _, hs = jax.lax.scan(cell, initial_state, xs)
        return jnp.swapaxes(hs, 0, 1)

    def _L0_ffn_ref(hidden_states, router_w, Wa, Wb):
        import jax, jax.numpy as jnp
        import numpy as np
        IN_F, OUT_F = (1024, 1024)
        N_EXPERTS, RANK, TOP_K = (8, 128, 2)
        B, S, D = hidden_states.shape
        x = hidden_states.reshape(-1, D)
        norm = jnp.maximum(jnp.linalg.norm(x, axis=-1, keepdims=True), 1e-12)
        router_logits = x / norm @ router_w
        routing_weights = jax.nn.softmax(router_logits.astype(jnp.float32), axis=-1)
        rw, selected_experts = jax.lax.top_k(routing_weights, TOP_K)
        rw = rw / jnp.sum(rw, axis=-1, keepdims=True)
        rw = rw.astype(hidden_states.dtype)
        combine = jnp.sum(jax.nn.one_hot(selected_experts, N_EXPERTS, dtype=rw.dtype) * rw[..., None], axis=1)
        out = jnp.zeros((x.shape[0], OUT_F), dtype=hidden_states.dtype)
        for e in range(N_EXPERTS):
            out = out + combine[:, e, None] * (x @ Wa[e] @ Wb[e])
        return out.reshape(B, S, OUT_F)
    x = x + _L0_ffn_ref(_L0_cond_ref(cond_2048, x, L0_cond_W_ih, L0_cond_W_hh, L0_cond_b_ih, L0_cond_b_hh), L0_ffn_router_w, L0_ffn_Wa, L0_ffn_Wb)
    return x

_drawn_inputs = setup_inputs


def setup_inputs(seed=0):
    import zlib

    import numpy as np

    out = dict(_drawn_inputs(seed))
    spreads = {'L0_cond_b_ih': (0.0, 0.1), 'L0_cond_b_hh': (0.0, 0.1)}
    factors = {'cond_2048': 2.833}
    for name, (base, spread) in spreads.items():
        noise = np.random.default_rng([zlib.crc32(name.encode()), seed]).standard_normal(out[name].shape)
        drawn = base * np.exp(spread * noise) if base else spread * noise
        out[name] = jnp.asarray(drawn.astype(out[name].dtype))
    for name, factor in factors.items():
        out[name] = (out[name] * factor).astype(out[name].dtype)
    return out
```

```python
import concourse.bass as bass
from concourse import mybir
from contextlib import ExitStack

FP32 = mybir.dt.float32
ALU = mybir.AluOpType
ACT = mybir.ActivationFunctionType
AX = mybir.AxisListType

P = 128
Q = 32
NQ = P // Q
GATES = 3
START = 1
DMA = 16



def input_projection(nc, x, w_ih, b_ih, b_hh, gi_dram):
    B, T, D = x.shape
    NC = D // P
    NM = GATES * NC
    TB = 64
    NB = T // TB
    TQ = TB // Q
    GW = D // NQ
    BANKS = 4
    with ExitStack() as ctx:
        def sb(name, shape):
            return ctx.enter_context(nc.sbuf_tensor(name, shape, FP32))

        def sem(name):
            return ctx.enter_context(nc.semaphore(name))

        w = sb("w_ih_sb", [P, NC, GATES * D])
        x_raw = [sb(f"x_raw{s}", [P, B, TQ, GW]) for s in range(2)]
        x_t = [sb(f"x_t{s}", [P, NC, B, TQ, Q]) for s in range(2)]
        stage = [sb(f"gi_stage{s}", [P, TB, NM, B]) for s in range(2)]
        bias = sb("gi_bias", [P, GATES, NC])
        bias_hh = sb("gi_bias_hh", [P, 2, NC])
        ps = [ctx.enter_context(nc.psum_tensor(f"gi_ps{n}", [P, 512], FP32)) for n in range(BANKS)]
        w_in = [sem(f"w_ih_in{q}") for q in range(GATES)]
        bias_in = sem("bias_in")
        bias_ready = sem("bias_ready")
        x_in = [sem(f"x_in{s}") for s in range(2)]
        xt_ready = sem("xt_ready")
        xt_read = [sem(f"xt_read{s}") for s in range(2)]
        mm_done = sem("gi_mm_done")
        bank_read = [sem(f"gi_bank_read{n}") for n in range(BANKS)]
        gi_out = [sem(f"gi_out{s}") for s in range(2)]
        block = ctx.enter_context(nc.Block())

        @block.sync
        def _(sp):
            def load_x(s, blk):
                for j in range(NQ):
                    for b in range(B):
                        src = x[b, bass.ds(blk * TB, TB), j * GW:(j + 1) * GW]
                        sp.dma_start(x_raw[s][j * Q:(j + 1) * Q, b, :, :],
                                     src.rearrange("(q i) f -> i q f", i=Q)).then_inc(x_in[s], DMA)

            def store_gi(s, blk, n):
                for k in range(BANKS):
                    sp.wait_ge(bank_read[k], START + (blk + 1) * (NM // BANKS))
                sp.dma_start(gi_dram[:, bass.ds(blk * TB, TB), :],
                             stage[s][:, :, :, :].rearrange("p t m b -> p t (m b)")).then_inc(gi_out[s], DMA)

            for s in range(2):
                sp.sem_inc(gi_out[s], DMA * START)
            load_x(0, 0)
            for q in range(GATES):
                for c in range(NC):
                    for j in range(NQ):
                        sp.dma_start(w[j * Q:(j + 1) * Q, c, q * D:(q + 1) * D],
                                     w_ih[j * GW + c * Q:j * GW + (c + 1) * Q, q * D:(q + 1) * D])\
                          .then_inc(w_in[q], DMA)
            load_x(1, 1)
            with sp.Fori(0, NB // 2 - 1) as n:
                for s in range(2):
                    sp.wait_ge(xt_ready, 2 * n + s + 1)
                    load_x(s, 2 * n + s + 2)
                    store_gi(s, 2 * n + s, n)
            for s in range(2):
                store_gi(s, NB - 2 + s, NB // 2 - 1)
            for s in range(2):
                sp.wait_ge(gi_out[s], DMA * (START + NB // 2))

        @block.gpsimd
        def _(pool):
            for q in range(GATES):
                pool.dma_start(bias[:, q, :], b_ih[q * D:(q + 1) * D].rearrange("(c p) -> p c", p=P),
                               allow_slow_non_contiguous=True).then_inc(bias_in, DMA)
                if q < 2:
                    pool.dma_start(bias_hh[:, q, :], b_hh[q * D:(q + 1) * D].rearrange("(c p) -> p c", p=P),
                                   allow_slow_non_contiguous=True).then_inc(bias_in, DMA)

        @block.vector
        def _(dve):
            dve.wait_ge(bias_in, DMA * (GATES + 2))
            nc.vector.tensor_tensor(bias[:, 0:2, :], bias[:, 0:2, :], bias_hh[:, :, :], ALU.add)\
              .then_inc(bias_ready, 1)
            with dve.Fori(0, NB // 2) as n:
                for s in range(2):
                    dve.wait_ge(x_in[s], (n + 1) * DMA * NQ * B)
                    dve.wait_ge(xt_read[s], START + n)
                    for b in range(B):
                        for q in range(TQ):
                            ins = nc.vector.transpose(
                                x_t[s][:, :, b, q, :],
                                x_raw[s][:, b, q, :].rearrange("p (c i) -> p c i", i=Q))
                    ins.then_inc(xt_ready, 1)

        @block.tensor
        def _(pe):
            for s in range(2):
                pe.sem_inc(xt_read[s], START)
            for q in range(GATES):
                pe.wait_ge(w_in[q], DMA * NC * NQ)
            with pe.Fori(0, NB // 2) as n:
                for s in range(2):
                    pe.wait_ge(xt_ready, 2 * n + s + 1)
                    for m in range(NM):
                        pe.wait_ge(bank_read[m % BANKS], START + (2 * n + s) * (NM // BANKS) + m // BANKS)
                        for c in range(NC):
                            ins = nc.tensor.matmul(
                                ps[m % BANKS][:, 0:B * TB], w[:, c, m * P:(m + 1) * P],
                                x_t[s][:, c, :, :, :].rearrange("p b q i -> p (b q i)"),
                                start=(c == 0), stop=(c == NC - 1))
                        ins.then_inc(mm_done, 1)
                    pe.wait_ge(mm_done, (2 * n + s + 1) * NM)
                    pe.sem_inc(xt_read[s], 1)

        @block.scalar
        def _(act):
            for k in range(BANKS):
                act.sem_inc(bank_read[k], START)
            act.wait_ge(bias_ready, 1)
            with act.Fori(0, NB // 2) as n:
                for s in range(2):
                    act.wait_ge(gi_out[s], DMA * (START + n))
                    for m in range(NM):
                        act.wait_ge(mm_done, (2 * n + s) * NM + m + 1)
                        nc.scalar.activation(
                            stage[s][:, :, m, :].rearrange("p t b -> p b t"),
                            ps[m % BANKS][:, 0:B * TB].rearrange("p (b t) -> p b t", b=B),
                            ACT.Identity, bias=bias[:, m // NC, m % NC:m % NC + 1])\
                          .then_inc(bank_read[m % BANKS], 1)


def recurrence(nc, h_start, w_hh, b_hh, gi_dram, hist_dram):
    T = gi_dram.shape[1]
    B, D = h_start.shape
    NC = D // P
    GW = D // NQ
    PARTS = [(0, 3), (3, NC)]
    SLOTS = 4
    CH = 2
    NI = T // SLOTS
    VOPS = 6
    with ExitStack() as ctx:
        def sb(name, shape):
            return ctx.enter_context(nc.sbuf_tensor(name, shape, FP32))

        def sem(name):
            return ctx.enter_context(nc.semaphore(name))

        w = sb("w_hh_sb", [P, NC, GATES * D])
        gi = [sb(f"gi{s}", [P, CH, GATES, NC, B]) for s in range(2)]
        h = sb("h", [P, SLOTS, NC, B])
        rows = sb("h_start_rows", [P, GW])
        rows_t = sb("h_start_t", [P, NC, Q])
        b_cand = sb("b_hh_candidate", [P, NC])
        gh = [sb(f"gh{k}", [P, GATES, c1 - c0, Q]) for k, (c0, c1) in enumerate(PARTS)]
        pre = [sb(f"pre{k}", [P, 2, c1 - c0, B]) for k, (c0, c1) in enumerate(PARTS)]
        gate = [sb(f"gate{k}", [P, 2, c1 - c0, B]) for k, (c0, c1) in enumerate(PARTS)]
        h_cand = [sb(f"h_cand{k}", [P, c1 - c0, B]) for k, (c0, c1) in enumerate(PARTS)]
        r_cand = [sb(f"r_cand{k}", [P, c1 - c0, B]) for k, (c0, c1) in enumerate(PARTS)]
        cand_in = [sb(f"cand_in{k}", [P, c1 - c0, B]) for k, (c0, c1) in enumerate(PARTS)]
        cand = [sb(f"cand{k}", [P, c1 - c0, B]) for k, (c0, c1) in enumerate(PARTS)]
        omz = [sb(f"one_minus_z{k}", [P, c1 - c0, B]) for k, (c0, c1) in enumerate(PARTS)]
        zh = [sb(f"zh{k}", [P, c1 - c0, B]) for k, (c0, c1) in enumerate(PARTS)]
        zn = [sb(f"zn{k}", [P, c1 - c0, B]) for k, (c0, c1) in enumerate(PARTS)]
        ps = [[ctx.enter_context(nc.psum_tensor(f"gh_ps{k}_{s}", [P, 512], FP32)) for s in range(2)]
              for k in range(2)]
        w_in = sem("w_hh_in")
        start_in = sem("start_in")
        b_in = sem("b_cand_in")
        cleared = sem("cleared")
        rows_cleared = sem("rows_cleared")
        start_t = sem("start_transposed")
        gi_in = [sem(f"gi_in{s}") for s in range(2)]
        hist_out = [sem(f"hist_out{s}") for s in range(2)]
        mm_done = [sem(f"gh_done{k}") for k in range(2)]
        h_ready = [sem(f"h_ready{k}") for k in range(2)]
        chain = sem("chain")
        pre_ready = sem("pre_ready")
        gate_ready = sem("gate_ready")
        cand_in_ready = sem("cand_in_ready")
        cand_ready = sem("cand_ready")
        block = ctx.enter_context(nc.Block())

        @block.sync
        def _(sp):
            def load_gi(s, t):
                sp.dma_start(gi[s][:, :, :, :, :].rearrange("p t q c b -> p t (q c b)"),
                             gi_dram[:, bass.ds(t, CH), :]).then_inc(gi_in[s], DMA)

            def store_h(s, t):
                sp.dma_start(hist_dram[:, bass.ds(t, CH), :],
                             h[:, CH * s:CH * (s + 1), :, :].rearrange("p t c b -> p t (c b)"))\
                  .then_inc(hist_out[s], DMA)

            for s in range(2):
                sp.sem_inc(hist_out[s], DMA * START)
            sp.wait_ge(rows_cleared, 1)
            for j in range(NQ):
                sp.dma_start(rows[j * Q:j * Q + B, :].rearrange("b (c i) -> b c i", i=Q),
                             h_start.rearrange("b (c j i) -> b j c i", j=NQ, i=Q)[:, j, :, :]).then_inc(start_in, DMA)
            for s in range(2):
                load_gi(s, CH * s)
            for c in range(NC):
                sp.dma_start(w[:, c, :], w_hh[c * P:(c + 1) * P, :]).then_inc(w_in, DMA)
            with sp.Fori(1, NI) as i:
                for s in range(2):
                    for k in range(2):
                        sp.wait_ge(h_ready[k], 1 + SLOTS * (i - 1) + CH * (s + 1))
                    store_h(s, SLOTS * (i - 1) + CH * s)
                    load_gi(s, SLOTS * i + CH * s)
            for s in range(2):
                for k in range(2):
                    sp.wait_ge(h_ready[k], 1 + SLOTS * (NI - 1) + CH * (s + 1))
                store_h(s, SLOTS * (NI - 1) + CH * s)
            for s in range(2):
                sp.wait_ge(hist_out[s], DMA * (START + NI))

        @block.gpsimd
        def _(pool):
            pool.dma_start(b_cand[:, :], b_hh[2 * D:3 * D].rearrange("(c p) -> p c", p=P),
                           allow_slow_non_contiguous=True).then_inc(b_in, DMA)

        @block.vector
        def _(dve):
            nc.vector.memset(rows[:, :], 0.0).then_inc(rows_cleared, 1)
            for k in range(2):
                for s in range(2):
                    nc.vector.memset(ps[k][s][:, :], 0.0).then_inc(cleared, 1)
            dve.wait_ge(start_in, DMA * NQ)
            nc.vector.transpose(rows_t[:, :, :], rows[:, :].rearrange("p (c i) -> p c i", i=Q)).then_inc(start_t, 1)
            dve.wait_ge(start_t, 1)
            for k, (c0, c1) in enumerate(PARTS):
                nc.vector.tensor_copy(h[:, SLOTS - 1, c0:c1, :], rows_t[:, c0:c1, 0:B]).then_inc(h_ready[k], 1)
            dve.wait_ge(b_in, DMA)

            def part(i, t, k):
                c0, c1 = PARTS[k]
                n = c1 - c0
                x_gates = gi[t // CH][:, t % CH, 0:2, c0:c1, :].rearrange("p q c b -> p q (c b)")
                x_cand = gi[t // CH][:, t % CH, 2, c0:c1, :]
                step = SLOTS * i + t
                links = (2 * step + k) * VOPS
                turns = 2 * step + k
                dve.wait_ge(mm_done[k], step + 1)
                nc.vector.transpose(
                    gh[k][:, :, :, :],
                    ps[k][t % 2][:, 0:GATES * n * Q].rearrange("p (q c i) -> p q c i", q=GATES, i=Q))\
                  .then_inc(chain, 1)
                if k == 0 and t % CH == 0:
                    dve.wait_ge(gi_in[t // CH], DMA * (i + 1))
                dve.wait_ge(chain, links + 1)
                nc.vector.tensor_tensor(pre[k][:, :, :, :], gh[k][:, 0:2, :, 0:B],
                                        x_gates.rearrange("p q (c b) -> p q c b", b=B), ALU.add)\
                  .then_inc(pre_ready, 1)
                nc.vector.tensor_tensor(h_cand[k][:, :, :], gh[k][:, 2, :, 0:B],
                                        b_cand[:, c0:c1].unsqueeze(2).broadcast_to([P, n, B]), ALU.add)\
                  .then_inc(chain, 1)
                dve.wait_ge(gate_ready, turns + 1)
                dve.wait_ge(chain, links + 2)
                nc.vector.tensor_tensor(r_cand[k][:, :, :], h_cand[k][:, :, :], gate[k][:, 0, :, :], ALU.mult)\
                  .then_inc(chain, 1)
                dve.wait_ge(chain, links + 3)
                nc.vector.tensor_tensor(cand_in[k][:, :, :], r_cand[k][:, :, :], x_cand, ALU.add)\
                  .then_inc(cand_in_ready, 1)
                nc.vector.tensor_scalar(omz[k][:, :, :], gate[k][:, 1, :, :], -1.0, 1.0, ALU.mult, ALU.add)\
                  .then_inc(chain, 1)
                nc.vector.tensor_tensor(zh[k][:, :, :], gate[k][:, 1, :, :], h[:, (t - 1) % SLOTS, c0:c1, :],
                                        ALU.mult).then_inc(chain, 1)
                dve.wait_ge(cand_ready, turns + 1)
                dve.wait_ge(chain, links + 4)
                nc.vector.tensor_tensor(zn[k][:, :, :], omz[k][:, :, :], cand[k][:, :, :], ALU.mult)\
                  .then_inc(chain, 1)
                if k == 0 and t % CH == 0:
                    dve.wait_ge(hist_out[t // CH], DMA * (START + i))
                dve.wait_ge(chain, links + 6)
                nc.vector.tensor_tensor(h[:, t, c0:c1, :], zn[k][:, :, :], zh[k][:, :, :], ALU.add)\
                  .then_inc(h_ready[k], 1)

            with dve.Fori(0, NI) as i:
                for t in range(SLOTS):
                    for k in range(2):
                        part(i, t, k)

        @block.scalar
        def _(act):
            with act.Fori(0, NI) as i:
                for t in range(SLOTS):
                    for k in range(2):
                        turns = 2 * (SLOTS * i + t) + k
                        act.wait_ge(pre_ready, turns + 1)
                        nc.scalar.activation(gate[k][:, :, :, :], pre[k][:, :, :, :], ACT.Sigmoid)\
                          .then_inc(gate_ready, 1)
                        act.wait_ge(cand_in_ready, turns + 1)
                        nc.scalar.activation(cand[k][:, :, :], cand_in[k][:, :, :], ACT.Tanh)\
                          .then_inc(cand_ready, 1)

        @block.tensor
        def _(pe):
            w_quarter = w[:, :, :].rearrange("p c (q k j i) -> p c j q k i", q=GATES, j=NQ, i=Q)

            def products(t, k_in, k_out):
                i0, i1 = PARTS[k_in]
                o0, o1 = PARTS[k_out]
                for c in range(i0, i1):
                    for j in range(NQ):
                        ins = nc.tensor.matmul(
                            ps[k_out][t % 2][j * Q:j * Q + B, 0:GATES * (o1 - o0) * Q],
                            h[:, (t - 1) % SLOTS, c, :], w_quarter[:, c, j, :, o0:o1, :],
                            start=(c == 0), stop=(c == NC - 1))
                return ins

            pe.wait_ge(cleared, 4)
            pe.wait_ge(w_in, DMA * NC)
            with pe.Fori(0, NI) as i:
                for t in range(SLOTS):
                    pe.wait_ge(h_ready[0], SLOTS * i + t + 1)
                    products(t, 0, 0)
                    products(t, 0, 1)
                    pe.wait_ge(h_ready[1], SLOTS * i + t + 1)
                    products(t, 1, 0).then_inc(mm_done[0], 1)
                    products(t, 1, 1).then_inc(mm_done[1], 1)


def routed_ffn(nc, x, hist_dram, router_w, w_a, w_b, out):
    B, T, D = x.shape
    E, _, R = w_a.shape
    NC = D // P
    GW = D // NQ
    TB = P
    NB = T // TB
    TOK = B * TB
    NH = D // 512
    TK = TB // Q
    KU, KB, KY = 3, 2, 2
    with ExitStack() as ctx:
        def sb(name, shape):
            return ctx.enter_context(nc.sbuf_tensor(name, shape, FP32))

        def pb(name):
            return ctx.enter_context(nc.psum_tensor(name, [P, 512], FP32))

        def sem(name):
            return ctx.enter_context(nc.semaphore(name))

        wa = sb("wa", [P, E, NC, R])
        wb = sb("wb", [P, E, D])
        h_raw = sb("h_raw", [P, TB, NC, B])
        ht = sb("ht", [P, NC, B, TB])
        hsq = sb("hsq", [P, NC, B, TB])
        x_nat = sb("x_nat", [P, B, D])
        us = sb("us", [P, E, B, TB])
        yo = [sb(f"y_out{s}", [P, 512]) for s in range(KY)]
        bcs = [sb(f"weight_of_expert{s}", [P, 512]) for s in range(KB)]
        rw = sb("router", [P, NC, Q])
        one_col = sb("one_col", [P, Q])
        sel = sb("sel", [P, E, P])
        lt = sb("logits_t", [P, TK, Q])
        low = sb("low", [P, E, E])
        half = sb("half", [P, TK])
        norm0 = sb("norm0", [P, TK])
        norm = sb("norm", [P, TK])
        rnorm = sb("rnorm", [P, TK])
        logit = sb("logit", [P, TK, E])
        top = sb("top", [P, TK])
        shifted = sb("shifted", [P, TK, E])
        expd = sb("expd", [P, TK, E])
        total = sb("total", [P, TK])
        rtotal = sb("rtotal", [P, TK])
        prob = sb("prob", [P, TK, E])
        above = sb("above", [P, TK, E, E])
        equal = sb("equal", [P, TK, E, E])
        before = sb("before", [P, TK, E, E])
        ahead = sb("ahead", [P, TK, E, E])
        rank = sb("rank", [P, TK, E])
        taken = sb("taken", [P, TK, E])
        kept = sb("kept", [P, TK, E])
        ksum = sb("ksum", [P, TK])
        rksum = sb("rksum", [P, TK])
        comb = sb("comb", [P, TK, Q])
        comb_t = sb("comb_t", [P, B, TB])
        ps_l = pb("ps_logits")
        ps_u = [pb(f"ps_u{s}") for s in range(KU)]
        ps_b = [pb(f"ps_b{s}") for s in range(KB)]
        ps_y = [pb(f"ps_y{s}") for s in range(KY)]
        consts = sem("consts")
        w_in = sem("ffn_w_in")
        rw_zero = sem("rw_zero")
        rw_in = sem("rw_in")
        sel_zero = sem("sel_zero")
        sel_ready = sem("sel_ready")
        h_in = sem("h_in")
        x_in = sem("x_nat_in")
        ht_ready = sem("ht_ready")
        hsq_ready = sem("hsq_ready")
        l_done = sem("logits_done")
        route = sem("route")
        norm_ready = sem("norm_ready")
        shifted_ready = sem("shifted_ready")
        exp_ready = sem("exp_ready")
        sumsq_ready = sem("sumsq_ready")
        comb_ready = sem("comb_ready")
        b_done = sem("broadcast_done")
        bcs_ready = sem("weight_ready")
        u_done = sem("hidden_done")
        us_ready = sem("scaled_ready")
        y_done = sem("y_done")
        yo_ready = sem("y_out_ready")
        y_out = [sem(f"y_out_dma{s}") for s in range(KY)]
        block = ctx.enter_context(nc.Block())
        ROUTE = 17
        NY = B * NH

        @block.sync
        def _(sp):
            def load(n):
                sp.dma_start(h_raw[:, :, :, :].rearrange("p t c b -> p t (c b)"),
                             hist_dram[:, bass.ds(n * TB, TB), :]).then_inc(h_in, DMA)

            for s in range(KY):
                sp.sem_inc(y_out[s], DMA * START)
            load(0)
            for e in range(E):
                sp.dma_start(wa[:, e, :, :], w_a[e, :, :].rearrange("(c p) r -> p c r", p=P)).then_inc(w_in, DMA)
            for e in range(E):
                sp.dma_start(wb[:, e, :], w_b[e, :, :]).then_inc(w_in, DMA)
            sp.wait_ge(rw_zero, 1)
            sp.dma_start(rw[:, :, 0:E], router_w.rearrange("(c p) e -> p c e", p=P),
                         allow_slow_non_contiguous=True).then_inc(rw_in, DMA)
            def outputs(n, last):
                if not last:
                    sp.wait_ge(ht_ready, B * (n + 1))
                    load(n + 1)
                sp.wait_ge(yo_ready, START + n * NY)
                sp.dma_start(x_nat[:, :, :], x[:, bass.ds(n * TB, TB), :].rearrange("b t d -> t b d"))\
                  .then_inc(x_in, DMA)
                for y in range(NY):
                    sp.wait_ge(yo_ready, START + n * NY + y + 1)
                    sp.dma_start(out[y // NH, bass.ds(n * TB, TB), (y % NH) * 512:(y % NH + 1) * 512],
                                 yo[y % KY][:, :]).then_inc(y_out[y % KY], DMA)

            with sp.Fori(0, NB - 1) as n:
                outputs(n, False)
            outputs(NB - 1, True)
            for s in range(KY):
                sp.wait_ge(y_out[s], DMA * (START + NB * NY // KY))

        @block.gpsimd
        def _(pool):
            pool.wait_ge(sel_zero, 2)
            for j in range(NQ):
                nc.gpsimd.affine_select(out=sel[:, :, :], in_=sel[:, :, :], compare_op=ALU.not_equal, fill=1.0,
                                        base=-Q * j, pattern=[[-1, E], [0, P]], channel_multiplier=1)\
                  .then_inc(sel_ready, 1)
                pool.wait_ge(sel_ready, j + 1)
            nc.gpsimd.affine_select(out=low[:, :, :], in_=low[:, :, :], compare_op=ALU.is_gt, fill=0.0,
                                    base=0, pattern=[[1, E], [-1, E]], channel_multiplier=0)\
              .then_inc(sel_ready, 1)
            with pool.Fori(0, NB) as n:
                pool.wait_ge(sumsq_ready, n + 1)
                nc.gpsimd.tensor_tensor(norm0[:, :], lt[:, :, E], half[:, :], ALU.pow).then_inc(norm_ready, 1)

        @block.scalar
        def _(act):
            act.sem_inc(bcs_ready, START)
            with act.Fori(0, NB) as n:
                act.wait_ge(h_in, DMA * (n + 1))
                act.wait_ge(u_done, START + n * E)
                for b in range(B):
                    nc.scalar.activation(ht[:, :, b, :], h_raw[:, :, :, b].rearrange("p t c -> p c t"),
                                         ACT.Copy).then_inc(ht_ready, 1)
                for b in range(B):
                    act.wait_ge(ht_ready, B * n + b + 1)
                    nc.scalar.activation(hsq[:, :, b, :], ht[:, :, b, :], ACT.Square).then_inc(hsq_ready, 1)
                act.wait_ge(shifted_ready, n + 1)
                nc.scalar.activation(expd[:, :, :], shifted[:, :, :], ACT.Exp).then_inc(exp_ready, 1)
                for e in range(E):
                    act.wait_ge(b_done, START + n * E + e + 1)
                    if e >= KB:
                        act.wait_ge(us_ready, START + n * E + e - KB + 1)
                    else:
                        act.wait_ge(us_ready, START + n * E)
                    nc.scalar.activation(bcs[e % KB][:, :], ps_b[e % KB][:, :], ACT.Copy).then_inc(bcs_ready, 1)

        @block.vector
        def _(dve):
            dve.sem_inc(us_ready, START)
            dve.sem_inc(yo_ready, START)
            nc.vector.memset(rw[:, :, :], 0.0).then_inc(rw_zero, 1)
            nc.vector.memset(sel[:, :, :], 0.0).then_inc(sel_zero, 1)
            nc.vector.memset(low[:, :, :], 1.0).then_inc(sel_zero, 1)
            nc.vector.memset(one_col[:, :], 0.0).then_inc(consts, 1)
            nc.vector.memset(half[:, :], 0.5).then_inc(consts, 1)
            nc.vector.memset(comb[:, :, :], 0.0).then_inc(consts, 1)
            nc.vector.memset(comb_t[:, :, :], 0.0).then_inc(consts, 1)
            dve.wait_ge(consts, 4)
            nc.vector.memset(one_col[:, E:E + 1], 1.0).then_inc(consts, 1)
            dve.wait_ge(sel_ready, NQ + 1)

            def wide(a):
                return a.unsqueeze(2).broadcast_to([P, TK, E])

            with dve.Fori(0, NB) as n:
                at = [0]

                def link(ins):
                    at[0] += 1
                    ins.then_inc(route, 1)
                    dve.wait_ge(route, n * ROUTE + at[0])

                dve.wait_ge(l_done, n + 1)
                nc.vector.transpose(lt[:, :, :], ps_l[:, 0:P].rearrange("p (k i) -> p k i", i=Q))\
                  .then_inc(sumsq_ready, 1)
                dve.wait_ge(norm_ready, n + 1)
                link(nc.vector.tensor_scalar(norm[:, :], norm0[:, :], 1e-12, None, ALU.max))
                link(nc.vector.reciprocal(rnorm[:, :], norm[:, :]))
                link(nc.vector.tensor_tensor(logit[:, :, :], lt[:, :, 0:E], wide(rnorm[:, :]), ALU.mult))
                link(nc.vector.tensor_reduce(top[:, :], logit[:, :, :], AX.X, ALU.max))
                nc.vector.tensor_tensor(shifted[:, :, :], logit[:, :, :], wide(top[:, :]), ALU.subtract)\
                  .then_inc(shifted_ready, 1)
                dve.wait_ge(exp_ready, n + 1)
                link(nc.vector.tensor_reduce(total[:, :], expd[:, :, :], AX.X, ALU.add))
                link(nc.vector.reciprocal(rtotal[:, :], total[:, :]))
                link(nc.vector.tensor_tensor(prob[:, :, :], expd[:, :, :], wide(rtotal[:, :]), ALU.mult))
                pe_ = prob[:, :, :].unsqueeze(3).broadcast_to([P, TK, E, E])
                pf_ = prob[:, :, :].unsqueeze(2).broadcast_to([P, TK, E, E])
                link(nc.vector.tensor_tensor(above[:, :, :, :], pf_, pe_, ALU.is_gt))
                link(nc.vector.tensor_tensor(equal[:, :, :, :], pf_, pe_, ALU.is_equal))
                link(nc.vector.tensor_tensor(before[:, :, :, :], equal[:, :, :, :],
                                             low[:, :, :].unsqueeze(1).broadcast_to([P, TK, E, E]), ALU.mult))
                link(nc.vector.tensor_tensor(ahead[:, :, :, :], before[:, :, :, :], above[:, :, :, :], ALU.add))
                link(nc.vector.tensor_reduce(rank[:, :, :], ahead[:, :, :, :], AX.X, ALU.add))
                link(nc.vector.tensor_scalar(taken[:, :, :], rank[:, :, :], 2.0, None, ALU.is_lt))
                link(nc.vector.tensor_tensor(kept[:, :, :], taken[:, :, :], prob[:, :, :], ALU.mult))
                link(nc.vector.tensor_reduce(ksum[:, :], kept[:, :, :], AX.X, ALU.add))
                link(nc.vector.reciprocal(rksum[:, :], ksum[:, :]))
                link(nc.vector.tensor_tensor(comb[:, :, 0:E], kept[:, :, :], wide(rksum[:, :]), ALU.mult))
                dve.wait_ge(b_done, START + n * E)
                for j in range(NQ):
                    ins = nc.vector.transpose(
                        comb_t[j * Q:(j + 1) * Q, j, :].rearrange("p (k i) -> p k i", i=Q),
                        comb[j * Q:(j + 1) * Q, :, :])
                ins.then_inc(comb_ready, 1)
                assert at[0] == ROUTE, at
                dve.wait_ge(y_done, START + n * NY)
                for e in range(E):
                    dve.wait_ge(u_done, START + n * E + e + 1)
                    dve.wait_ge(bcs_ready, START + n * E + e + 1)
                    nc.vector.tensor_tensor(us[:, e, :, :].rearrange("p b t -> p (b t)"), ps_u[e % KU][:, :],
                                            bcs[e % KB][:, :], ALU.mult).then_inc(us_ready, 1)
                dve.wait_ge(x_in, DMA * (n + 1))
                for y in range(NY):
                    dve.wait_ge(y_done, START + n * NY + y + 1)
                    dve.wait_ge(y_out[y % KY], DMA * (START + n * (NY // KY) + y // KY))
                    nc.vector.tensor_tensor(yo[y % KY][:, :], ps_y[y % KY][:, :],
                                            x_nat[:, y // NH, (y % NH) * 512:(y % NH + 1) * 512], ALU.add)\
                      .then_inc(yo_ready, 1)

        @block.tensor
        def _(pe):
            for s in (u_done, b_done, y_done):
                pe.sem_inc(s, START)
            pe.wait_ge(consts, 5)
            pe.wait_ge(rw_in, DMA)
            pe.wait_ge(sel_ready, NQ + 1)
            pe.wait_ge(w_in, DMA * E * 2)
            with pe.Fori(0, NB) as n:
                def hidden(e):
                    if e >= KU:
                        pe.wait_ge(us_ready, START + n * E + e - KU + 1)
                    else:
                        pe.wait_ge(us_ready, START + n * E)
                    for c in range(NC):
                        ins = nc.tensor.matmul(ps_u[e % KU][:, :], wa[:, e, c, :],
                                               ht[:, c, :, :].rearrange("p b t -> p (b t)"),
                                               start=(c == 0), stop=(c == NC - 1))
                    ins.then_inc(u_done, 1)

                def broadcast(e):
                    if e >= KB:
                        pe.wait_ge(bcs_ready, START + n * E + e - KB + 1)
                    else:
                        pe.wait_ge(bcs_ready, START + n * E)
                    nc.tensor.matmul(ps_b[e % KB][:, :], sel[:, e, :],
                                     comb_t[:, :, :].rearrange("p b t -> p (b t)"),
                                     start=True, stop=True).then_inc(b_done, 1)

                pe.wait_ge(ht_ready, B * (n + 1))
                for c in range(NC):
                    for b in range(B):
                        nc.tensor.matmul(ps_l[b * Q:(b + 1) * Q, 0:TB], rw[:, c, :], ht[:, c, b, :],
                                         start=(c == 0), stop=False)
                pe.wait_ge(hsq_ready, B * (n + 1))
                for c in range(NC):
                    for b in range(B):
                        ins = nc.tensor.matmul(ps_l[b * Q:(b + 1) * Q, 0:TB], one_col[:, :], hsq[:, c, b, :],
                                               start=False, stop=(c == NC - 1))
                ins.then_inc(l_done, 1)
                hidden(0)
                hidden(1)
                pe.wait_ge(comb_ready, n + 1)
                broadcast(0)
                for e in range(2, E):
                    broadcast(e - 1)
                    hidden(e)
                broadcast(E - 1)
                for y in range(NY):
                    b, hf = y // NH, y % NH
                    for e in range(E):
                        pe.wait_ge(us_ready, START + n * E + e + 1)
                        if y < KY and e == 0:
                            pe.wait_ge(yo_ready, START + n * NY)
                        elif e == 0:
                            pe.wait_ge(yo_ready, START + n * NY + y - KY + 1)
                        ins = nc.tensor.matmul(ps_y[y % KY][:, :], us[:, e, b, :], wb[:, e, hf * 512:(hf + 1) * 512],
                                               start=(e == 0), stop=(e == E - 1))
                    ins.then_inc(y_done, 1)


def build(nc, x, h_start, w_ih, w_hh, b_ih, b_hh, router_w, w_a, w_b, out):
    B, T, D = x.shape
    gi_dram = nc.dram_tensor("gi_scratch", [P, T, GATES * D // P * B], FP32, kind="Internal").ap()
    hist_dram = nc.dram_tensor("h_scratch", [P, T, D // P * B], FP32, kind="Internal").ap()
    input_projection(nc, x, w_ih, b_ih, b_hh, gi_dram)
    recurrence(nc, h_start, w_hh, b_hh, gi_dram, hist_dram)
    routed_ffn(nc, x, hist_dram, router_w, w_a, w_b, out)


_INS = ['x', 'cond_2048', 'L0_cond_W_ih', 'L0_cond_W_hh', 'L0_cond_b_ih', 'L0_cond_b_hh',
        'L0_ffn_router_w', 'L0_ffn_Wa', 'L0_ffn_Wb']


def kernel(**inputs):
    import numpy as _np
    import concourse.bacc as _bacc
    from concourse import mybir as _mybir
    from concourse.bass_utils import run_bass_kernel_spmd as _run

    nc = _bacc.Bacc("TRN2", target_bir_lowering=False, num_devices=1)
    arrays, args = {}, []
    for name in _INS:
        a = _np.ascontiguousarray(inputs[name])
        arrays[f"in_{name}"] = a
        args.append(nc.dram_tensor(f"in_{name}", a.shape, _mybir.dt.from_np(a.dtype), kind="ExternalInput").ap())
    shape = inputs['x'].shape
    args.append(nc.dram_tensor("out", shape, _mybir.dt.float32, kind="ExternalOutput").ap())
    build(nc, *args)
    r = _run(nc, [arrays], core_ids=[0])
    return r.results[0]["out"]
```

```python
import concourse.bass as bass
from concourse import mybir
from contextlib import ExitStack

FP32 = mybir.dt.float32
BF16 = mybir.dt.bfloat16
ALU = mybir.AluOpType
ACT = mybir.ActivationFunctionType
AX = mybir.AxisListType

P = 128
Q = 32
NQ = P // Q
GATES = 3
START = 1
DMA = 16
SPLIT = 3



def input_projection(nc, x, w_ih, b_ih, b_hh, gi_dram):
    B, T, D = x.shape
    NC = D // P
    NM = GATES * NC
    TB = 64
    NB = T // TB
    TQ = TB // Q
    GW = D // NQ
    BANKS = 4
    with ExitStack() as ctx:
        def sb(name, shape):
            return ctx.enter_context(nc.sbuf_tensor(name, shape, FP32))

        def sem(name):
            return ctx.enter_context(nc.semaphore(name))

        w = sb("w_ih_sb", [P, NC, GATES * D])
        x_raw = [sb(f"x_raw{s}", [P, B, TQ, GW]) for s in range(2)]
        x_t = [sb(f"x_t{s}", [P, NC, B, TQ, Q]) for s in range(2)]
        stage = [sb(f"gi_stage{s}", [P, TB, NM, B]) for s in range(2)]
        bias = sb("gi_bias", [P, GATES, NC])
        bias_hh = sb("gi_bias_hh", [P, 2, NC])
        ps = [ctx.enter_context(nc.psum_tensor(f"gi_ps{n}", [P, 512], FP32)) for n in range(BANKS)]
        w_in = [sem(f"w_ih_in{q}") for q in range(GATES)]
        bias_in = sem("bias_in")
        bias_ready = sem("bias_ready")
        x_in = [sem(f"x_in{s}") for s in range(2)]
        xt_ready = sem("xt_ready")
        xt_read = [sem(f"xt_read{s}") for s in range(2)]
        mm_done = sem("gi_mm_done")
        bank_read = [sem(f"gi_bank_read{n}") for n in range(BANKS)]
        gi_out = [sem(f"gi_out{s}") for s in range(2)]
        block = ctx.enter_context(nc.Block())

        @block.sync
        def _(sp):
            def load_x(s, blk):
                for j in range(NQ):
                    for b in range(B):
                        src = x[b, bass.ds(blk * TB, TB), j * GW:(j + 1) * GW]
                        sp.dma_start(x_raw[s][j * Q:(j + 1) * Q, b, :, :],
                                     src.rearrange("(q i) f -> i q f", i=Q)).then_inc(x_in[s], DMA)

            def store_gi(s, blk, n):
                for k in range(BANKS):
                    sp.wait_ge(bank_read[k], START + (blk + 1) * (NM // BANKS))
                sp.dma_start(gi_dram[:, bass.ds(blk * TB, TB), :],
                             stage[s][:, :, :, :].rearrange("p t m b -> p t (m b)")).then_inc(gi_out[s], DMA)

            for s in range(2):
                sp.sem_inc(gi_out[s], DMA * START)
            load_x(0, 0)
            for q in range(GATES):
                for j in range(NQ):
                    sp.dma_start(w[j * Q:(j + 1) * Q, :, q * D:(q + 1) * D],
                                 w_ih[j * GW:(j + 1) * GW, q * D:(q + 1) * D].rearrange("(c i) n -> i c n", i=Q))\
                      .then_inc(w_in[q], DMA)
            load_x(1, 1)
            with sp.Fori(0, NB // 2 - 1) as n:
                for s in range(2):
                    sp.wait_ge(xt_ready, 2 * n + s + 1)
                    load_x(s, 2 * n + s + 2)
                    store_gi(s, 2 * n + s, n)
            for s in range(2):
                store_gi(s, NB - 2 + s, NB // 2 - 1)
            for s in range(2):
                sp.wait_ge(gi_out[s], DMA * (START + NB // 2))

        @block.gpsimd
        def _(pool):
            for q in range(GATES):
                pool.dma_start(bias[:, q, :], b_ih[q * D:(q + 1) * D].rearrange("(c p) -> p c", p=P),
                               allow_slow_non_contiguous=True).then_inc(bias_in, DMA)
                if q < 2:
                    pool.dma_start(bias_hh[:, q, :], b_hh[q * D:(q + 1) * D].rearrange("(c p) -> p c", p=P),
                                   allow_slow_non_contiguous=True).then_inc(bias_in, DMA)

        @block.vector
        def _(dve):
            dve.wait_ge(bias_in, DMA * (GATES + 2))
            nc.vector.tensor_tensor(bias[:, 0:2, :], bias[:, 0:2, :], bias_hh[:, :, :], ALU.add)\
              .then_inc(bias_ready, 1)
            with dve.Fori(0, NB // 2) as n:
                for s in range(2):
                    dve.wait_ge(x_in[s], (n + 1) * DMA * NQ * B)
                    dve.wait_ge(xt_read[s], START + n)
                    for b in range(B):
                        for q in range(TQ):
                            ins = nc.vector.transpose(
                                x_t[s][:, :, b, q, :],
                                x_raw[s][:, b, q, :].rearrange("p (c i) -> p c i", i=Q))
                    ins.then_inc(xt_ready, 1)

        @block.tensor
        def _(pe):
            for s in range(2):
                pe.sem_inc(xt_read[s], START)
            with pe.Fori(0, NB // 2) as n:
                for s in range(2):
                    pe.wait_ge(xt_ready, 2 * n + s + 1)
                    for m in range(NM):
                        if m % NC == 0:
                            pe.wait_ge(w_in[m // NC], DMA * NQ)
                        pe.wait_ge(bank_read[m % BANKS], START + (2 * n + s) * (NM // BANKS) + m // BANKS)
                        for c in range(NC):
                            ins = nc.tensor.matmul(
                                ps[m % BANKS][:, 0:B * TB], w[:, c, m * P:(m + 1) * P],
                                x_t[s][:, c, :, :, :].rearrange("p b q i -> p (b q i)"),
                                start=(c == 0), stop=(c == NC - 1))
                        ins.then_inc(mm_done, 1)
                    pe.wait_ge(mm_done, (2 * n + s + 1) * NM)
                    pe.sem_inc(xt_read[s], 1)

        @block.scalar
        def _(act):
            for k in range(BANKS):
                act.sem_inc(bank_read[k], START)
            act.wait_ge(bias_ready, 1)
            with act.Fori(0, NB // 2) as n:
                for s in range(2):
                    act.wait_ge(gi_out[s], DMA * (START + n))
                    for m in range(NM):
                        act.wait_ge(mm_done, (2 * n + s) * NM + m + 1)
                        nc.scalar.activation(
                            stage[s][:, :, m, :].rearrange("p t b -> p b t"),
                            ps[m % BANKS][:, 0:B * TB].rearrange("p (b t) -> p b t", b=B),
                            ACT.Identity, bias=bias[:, m // NC, m % NC:m % NC + 1])\
                          .then_inc(bank_read[m % BANKS], 1)


def recurrence(nc, h_start, w_hh, b_hh, gi_dram, hist_dram):
    T = gi_dram.shape[1]
    B, D = h_start.shape
    NC = D // P
    GW = D // NQ
    PARTS = [(0, 3), (3, NC)]
    SLOTS = 4
    CH = 2
    NI = T // SLOTS
    PW = GATES * D // 2
    PIECES = 2 * NC
    RAW = 4
    VOPS = 10
    with ExitStack() as ctx:
        def sb(name, shape):
            return ctx.enter_context(nc.sbuf_tensor(name, shape, FP32))

        def sem(name):
            return ctx.enter_context(nc.semaphore(name))

        w = ctx.enter_context(nc.sbuf_tensor("w_hh_parts", [P, SPLIT, NC, GATES * D], BF16))
        w_raw = [sb(f"w_hh_raw{s}", [P, PW]) for s in range(RAW)]
        w_rest = [sb(f"w_hh_rest{s}", [P, PW]) for s in range(2)]
        gi = [sb(f"gi{s}", [P, CH, GATES, NC, B]) for s in range(2)]
        h = sb("h", [P, SLOTS, NC, B])
        h_parts = ctx.enter_context(nc.sbuf_tensor("h_parts", [P, 2, NC, SPLIT, B], BF16))
        rows = sb("h_start_rows", [P, GW])
        rows_t = sb("h_start_t", [P, NC, Q])
        b_cand = sb("b_hh_candidate", [P, NC])
        gh = [sb(f"gh{k}", [P, GATES, c1 - c0, Q]) for k, (c0, c1) in enumerate(PARTS)]
        pre = [sb(f"pre{k}", [P, 2, c1 - c0, B]) for k, (c0, c1) in enumerate(PARTS)]
        gate = [sb(f"gate{k}", [P, 2, c1 - c0, B]) for k, (c0, c1) in enumerate(PARTS)]
        h_cand = [sb(f"h_cand{k}", [P, c1 - c0, B]) for k, (c0, c1) in enumerate(PARTS)]
        r_cand = [sb(f"r_cand{k}", [P, c1 - c0, B]) for k, (c0, c1) in enumerate(PARTS)]
        gh_sum = [sb(f"gh_sum{k}", [P, GATES, c1 - c0, B]) for k, (c0, c1) in enumerate(PARTS)]
        h_rest = [sb(f"h_rest{k}", [P, c1 - c0, B]) for k, (c0, c1) in enumerate(PARTS)]
        cand_in = [sb(f"cand_in{k}", [P, c1 - c0, B]) for k, (c0, c1) in enumerate(PARTS)]
        cand = [sb(f"cand{k}", [P, c1 - c0, B]) for k, (c0, c1) in enumerate(PARTS)]
        omz = [sb(f"one_minus_z{k}", [P, c1 - c0, B]) for k, (c0, c1) in enumerate(PARTS)]
        zh = [sb(f"zh{k}", [P, c1 - c0, B]) for k, (c0, c1) in enumerate(PARTS)]
        zn = [sb(f"zn{k}", [P, c1 - c0, B]) for k, (c0, c1) in enumerate(PARTS)]
        ps = [[ctx.enter_context(nc.psum_tensor(f"gh_ps{k}_{s}", [P, 512], FP32)) for s in range(2)]
              for k in range(2)]
        w_in = [sem(f"w_hh_in{s}") for s in range(RAW)]
        w_high = sem("w_high_ready")
        w_rest_ready = sem("w_rest_ready")
        w_middle = sem("w_middle_ready")
        w_low = sem("w_low_ready")
        start_in = sem("start_in")
        b_in = sem("b_cand_in")
        cleared = sem("cleared")
        rows_cleared = sem("rows_cleared")
        start_t = sem("start_transposed")
        gi_in = [sem(f"gi_in{s}") for s in range(2)]
        hist_out = [sem(f"hist_out{s}") for s in range(2)]
        mm_done = [sem(f"gh_done{k}") for k in range(2)]
        h_ready = [sem(f"h_ready{k}") for k in range(2)]
        parts_ready = [sem(f"h_parts_ready{k}") for k in range(2)]
        chain = sem("chain")
        pre_ready = sem("pre_ready")
        gate_ready = sem("gate_ready")
        cand_in_ready = sem("cand_in_ready")
        cand_ready = sem("cand_ready")
        block = ctx.enter_context(nc.Block())

        def piece(source, n):
            return source[n // 2 * P:(n // 2 + 1) * P, n % 2 * PW:(n % 2 + 1) * PW]

        def w_part(s, n):
            return w[:, s, n // 2, n % 2 * PW:(n % 2 + 1) * PW]

        @block.sync
        def _(sp):
            def load_gi(s, t):
                sp.dma_start(gi[s][:, :, :, :, :].rearrange("p t q c b -> p t (q c b)"),
                             gi_dram[:, bass.ds(t, CH), :]).then_inc(gi_in[s], DMA)

            def store_h(s, t):
                sp.dma_start(hist_dram[:, bass.ds(t, CH), :],
                             h[:, CH * s:CH * (s + 1), :, :].rearrange("p t c b -> p t (c b)"))\
                  .then_inc(hist_out[s], DMA)

            for s in range(2):
                sp.sem_inc(hist_out[s], DMA * START)
            sp.wait_ge(rows_cleared, 1)
            for j in range(NQ):
                sp.dma_start(rows[j * Q:j * Q + B, :].rearrange("b (c i) -> b c i", i=Q),
                             h_start.rearrange("b (c j i) -> b j c i", j=NQ, i=Q)[:, j, :, :]).then_inc(start_in, DMA)
            for s in range(2):
                load_gi(s, CH * s)
            for n in range(PIECES):
                if n >= RAW:
                    sp.wait_ge(w_high, n - RAW + 1)
                    sp.wait_ge(w_rest_ready, n - RAW + 1)
                sp.dma_start(w_raw[n % RAW][:, :], piece(w_hh, n)).then_inc(w_in[n % RAW], DMA)
            with sp.Fori(1, NI) as i:
                for s in range(2):
                    for k in range(2):
                        sp.wait_ge(h_ready[k], 1 + SLOTS * (i - 1) + CH * (s + 1))
                    store_h(s, SLOTS * (i - 1) + CH * s)
                    load_gi(s, SLOTS * i + CH * s)
            for s in range(2):
                for k in range(2):
                    sp.wait_ge(h_ready[k], 1 + SLOTS * (NI - 1) + CH * (s + 1))
                store_h(s, SLOTS * (NI - 1) + CH * s)
            for s in range(2):
                sp.wait_ge(hist_out[s], DMA * (START + NI))

        @block.gpsimd
        def _(pool):
            pool.dma_start(b_cand[:, :], b_hh[2 * D:3 * D].rearrange("(c p) -> p c", p=P),
                           allow_slow_non_contiguous=True).then_inc(b_in, DMA)

        @block.vector
        def _(dve):
            nc.vector.memset(rows[:, :], 0.0).then_inc(rows_cleared, 1)
            for k in range(2):
                for s in range(2):
                    nc.vector.memset(ps[k][s][:, :], 0.0).then_inc(cleared, 1)
            dve.wait_ge(start_in, DMA * NQ)
            nc.vector.transpose(rows_t[:, :, :], rows[:, :].rearrange("p (c i) -> p c i", i=Q)).then_inc(start_t, 1)
            dve.wait_ge(start_t, 1)
            for k, (c0, c1) in enumerate(PARTS):
                nc.vector.tensor_copy(h[:, SLOTS - 1, c0:c1, :], rows_t[:, c0:c1, 0:B]).then_inc(h_ready[k], 1)
                nc.vector.tensor_copy(h_parts[:, 1, c0:c1, 0, :], rows_t[:, c0:c1, 0:B]).then_inc(start_t, 1)
                dve.wait_ge(h_ready[k], 1)
                dve.wait_ge(start_t, 3 * k + 2)
                nc.vector.tensor_tensor(h_rest[k][:, :, :], h[:, SLOTS - 1, c0:c1, :],
                                        h_parts[:, 1, c0:c1, 0, :], ALU.subtract).then_inc(start_t, 1)
                nc.vector.tensor_tensor(h_parts[:, 1, c0:c1, 1, :], h[:, SLOTS - 1, c0:c1, :],
                                        h_parts[:, 1, c0:c1, 0, :], ALU.subtract).then_inc(start_t, 1)
                dve.wait_ge(start_t, 3 * k + 4)
                nc.vector.tensor_tensor(h_parts[:, 1, c0:c1, 2, :], h_rest[k][:, :, :],
                                        h_parts[:, 1, c0:c1, 1, :], ALU.subtract).then_inc(parts_ready[k], 1)
            dve.wait_ge(b_in, DMA)
            for n in range(PIECES + 1):
                if n < PIECES:
                    dve.wait_ge(w_high, n + 1)
                    if n >= 2:
                        dve.wait_ge(w_low, n - 1)
                    nc.vector.tensor_tensor(w_rest[n % 2][:, :], w_raw[n % RAW][:, :], w_part(0, n), ALU.subtract)\
                      .then_inc(w_rest_ready, 1)
                if n:
                    dve.wait_ge(w_middle, n)
                    nc.vector.tensor_tensor(w_part(2, n - 1), w_rest[(n - 1) % 2][:, :], w_part(1, n - 1),
                                            ALU.subtract).then_inc(w_low, 1)

            def part(i, t, k):
                c0, c1 = PARTS[k]
                n = c1 - c0
                x_gates = gi[t // CH][:, t % CH, 0:2, c0:c1, :].rearrange("p q c b -> p q (c b)")
                x_cand = gi[t // CH][:, t % CH, 2, c0:c1, :]
                step = SLOTS * i + t
                links = (2 * step + k) * VOPS
                turns = 2 * step + k
                dve.wait_ge(mm_done[k], step + 1)
                nc.vector.transpose(
                    gh[k][:, :, :, :],
                    ps[k][t % 2][:, 0:GATES * n * Q].rearrange("p (q c i) -> p q c i", q=GATES, i=Q))\
                  .then_inc(chain, 1)
                dve.wait_ge(chain, links + 1)
                nc.vector.tensor_reduce(
                    gh_sum[k][:, :, :, :].rearrange("p q c b -> p (q c) b"),
                    gh[k][:, :, :, 0:SPLIT * B].rearrange("p q c (s b) -> p (q c) b s", b=B),
                    AX.X, ALU.add).then_inc(chain, 1)
                if k == 0 and t % CH == 0:
                    dve.wait_ge(gi_in[t // CH], DMA * (i + 1))
                dve.wait_ge(chain, links + 2)
                nc.vector.tensor_tensor(pre[k][:, :, :, :], gh_sum[k][:, 0:2, :, :],
                                        x_gates.rearrange("p q (c b) -> p q c b", b=B), ALU.add)\
                  .then_inc(pre_ready, 1)
                nc.vector.tensor_tensor(h_cand[k][:, :, :], gh_sum[k][:, 2, :, :],
                                        b_cand[:, c0:c1].unsqueeze(2).broadcast_to([P, n, B]), ALU.add)\
                  .then_inc(chain, 1)
                dve.wait_ge(gate_ready, turns + 1)
                dve.wait_ge(chain, links + 3)
                nc.vector.tensor_tensor(r_cand[k][:, :, :], h_cand[k][:, :, :], gate[k][:, 0, :, :], ALU.mult)\
                  .then_inc(chain, 1)
                dve.wait_ge(chain, links + 4)
                nc.vector.tensor_tensor(cand_in[k][:, :, :], r_cand[k][:, :, :], x_cand, ALU.add)\
                  .then_inc(cand_in_ready, 1)
                nc.vector.tensor_scalar(omz[k][:, :, :], gate[k][:, 1, :, :], -1.0, 1.0, ALU.mult, ALU.add)\
                  .then_inc(chain, 1)
                nc.vector.tensor_tensor(zh[k][:, :, :], gate[k][:, 1, :, :], h[:, (t - 1) % SLOTS, c0:c1, :],
                                        ALU.mult).then_inc(chain, 1)
                dve.wait_ge(cand_ready, turns + 1)
                dve.wait_ge(chain, links + 5)
                nc.vector.tensor_tensor(zn[k][:, :, :], omz[k][:, :, :], cand[k][:, :, :], ALU.mult)\
                  .then_inc(chain, 1)
                if k == 0 and t % CH == 0:
                    dve.wait_ge(hist_out[t // CH], DMA * (START + i))
                dve.wait_ge(chain, links + 7)
                nc.vector.tensor_tensor(h_parts[:, t % 2, c0:c1, 0, :], zn[k][:, :, :], zh[k][:, :, :], ALU.add)\
                  .then_inc(chain, 1)
                nc.vector.tensor_tensor(h[:, t, c0:c1, :], zn[k][:, :, :], zh[k][:, :, :], ALU.add)\
                  .then_inc(h_ready[k], 1)
                dve.wait_ge(chain, links + 8)
                dve.wait_ge(h_ready[k], 2 + step)
                nc.vector.tensor_tensor(h_parts[:, t % 2, c0:c1, 1, :], h[:, t, c0:c1, :],
                                        h_parts[:, t % 2, c0:c1, 0, :], ALU.subtract).then_inc(chain, 1)
                nc.vector.tensor_tensor(h_rest[k][:, :, :], h[:, t, c0:c1, :],
                                        h_parts[:, t % 2, c0:c1, 0, :], ALU.subtract).then_inc(chain, 1)
                dve.wait_ge(chain, links + 10)
                nc.vector.tensor_tensor(h_parts[:, t % 2, c0:c1, 2, :], h_rest[k][:, :, :],
                                        h_parts[:, t % 2, c0:c1, 1, :], ALU.subtract).then_inc(parts_ready[k], 1)

            with dve.Fori(0, NI) as i:
                for t in range(SLOTS):
                    for k in range(2):
                        part(i, t, k)

        @block.scalar
        def _(act):
            for n in range(PIECES + 1):
                if n < PIECES:
                    act.wait_ge(w_in[n % RAW], DMA * (n // RAW + 1))
                    nc.scalar.activation(w_part(0, n), w_raw[n % RAW][:, :], ACT.Copy).then_inc(w_high, 1)
                if n:
                    act.wait_ge(w_rest_ready, n)
                    nc.scalar.activation(w_part(1, n - 1), w_rest[(n - 1) % 2][:, :], ACT.Copy)\
                      .then_inc(w_middle, 1)
            with act.Fori(0, NI) as i:
                for t in range(SLOTS):
                    for k in range(2):
                        turns = 2 * (SLOTS * i + t) + k
                        act.wait_ge(pre_ready, turns + 1)
                        nc.scalar.activation(gate[k][:, :, :, :], pre[k][:, :, :, :], ACT.Sigmoid)\
                          .then_inc(gate_ready, 1)
                        act.wait_ge(cand_in_ready, turns + 1)
                        nc.scalar.activation(cand[k][:, :, :], cand_in[k][:, :, :], ACT.Tanh)\
                          .then_inc(cand_ready, 1)

        @block.tensor
        def _(pe):
            w_quarter = [w[:, s, :, :].rearrange("p c (q k j i) -> p c j q k i", q=GATES, j=NQ, i=Q)
                         for s in range(SPLIT)]

            def products(t, k_in, k_out):
                i0, i1 = PARTS[k_in]
                o0, o1 = PARTS[k_out]
                for c in range(i0, i1):
                    for s in range(SPLIT):
                        for j in range(NQ):
                            ins = nc.tensor.matmul(
                                ps[k_out][t % 2][j * Q:j * Q + SPLIT * B, 0:GATES * (o1 - o0) * Q],
                                h_parts[:, (t - 1) % 2, c, :, :].rearrange("p s b -> p (s b)"),
                                w_quarter[s][:, c, j, :, o0:o1, :],
                                start=(c == 0 and s == 0), stop=(c == NC - 1 and s == SPLIT - 1))
                return ins

            pe.wait_ge(cleared, 4)
            pe.wait_ge(w_low, PIECES)
            with pe.Fori(0, NI) as i:
                for t in range(SLOTS):
                    pe.wait_ge(parts_ready[0], SLOTS * i + t + 1)
                    products(t, 0, 0)
                    products(t, 0, 1)
                    pe.wait_ge(parts_ready[1], SLOTS * i + t + 1)
                    products(t, 1, 0).then_inc(mm_done[0], 1)
                    products(t, 1, 1).then_inc(mm_done[1], 1)


def routed_ffn(nc, x, hist_dram, router_w, w_a, w_b, out):
    B, T, D = x.shape
    E, _, R = w_a.shape
    NC = D // P
    GW = D // NQ
    TB = P
    NB = T // TB
    TOK = B * TB
    NH = D // 512
    TK = TB // Q
    KU, KB, KY = 3, 2, 2
    with ExitStack() as ctx:
        def sb(name, shape):
            return ctx.enter_context(nc.sbuf_tensor(name, shape, FP32))

        def pb(name):
            return ctx.enter_context(nc.psum_tensor(name, [P, 512], FP32))

        def sem(name):
            return ctx.enter_context(nc.semaphore(name))

        wa = sb("wa", [P, E, NC, R])
        wb = sb("wb", [P, E, D])
        h_raw = sb("h_raw", [P, TB, NC, B])
        ht = sb("ht", [P, NC, B, TB])
        hsq = sb("hsq", [P, NC, B, TB])
        x_nat = sb("x_nat", [P, B, D])
        us = sb("us", [P, E, B, TB])
        yo = [sb(f"y_out{s}", [P, 512]) for s in range(KY)]
        bcs = [sb(f"weight_of_expert{s}", [P, 512]) for s in range(KB)]
        rw = sb("router", [P, NC, Q])
        one_col = sb("one_col", [P, Q])
        sel = ctx.enter_context(nc.sbuf_tensor("sel", [P, E, P], BF16))
        lt = sb("logits_t", [P, TK, Q])
        low = sb("low", [P, E, E])
        half = sb("half", [P, TK])
        norm0 = sb("norm0", [P, TK])
        norm = sb("norm", [P, TK])
        rnorm = sb("rnorm", [P, TK])
        logit = sb("logit", [P, TK, E])
        top = sb("top", [P, TK])
        shifted = sb("shifted", [P, TK, E])
        expd = sb("expd", [P, TK, E])
        total = sb("total", [P, TK])
        rtotal = sb("rtotal", [P, TK])
        prob = sb("prob", [P, TK, E])
        above = sb("above", [P, TK, E, E])
        equal = sb("equal", [P, TK, E, E])
        before = sb("before", [P, TK, E, E])
        ahead = sb("ahead", [P, TK, E, E])
        rank = sb("rank", [P, TK, E])
        taken = sb("taken", [P, TK, E])
        kept = sb("kept", [P, TK, E])
        ksum = sb("ksum", [P, TK])
        rksum = sb("rksum", [P, TK])
        comb = sb("comb", [P, TK, E])
        comb_rest = sb("comb_rest", [P, TK, E])
        comb_parts = ctx.enter_context(nc.sbuf_tensor("comb_parts", [P, TK, Q], BF16))
        comb_t = ctx.enter_context(nc.sbuf_tensor("comb_t", [P, B, TB], BF16))
        ps_l = pb("ps_logits")
        ps_u = [pb(f"ps_u{s}") for s in range(KU)]
        ps_b = [pb(f"ps_b{s}") for s in range(KB)]
        ps_y = [pb(f"ps_y{s}") for s in range(KY)]
        consts = sem("consts")
        wa_in = [sem(f"wa_in{e}") for e in range(E)]
        wb_in = sem("wb_in")
        rw_zero = sem("rw_zero")
        rw_in = sem("rw_in")
        sel_zero = sem("sel_zero")
        sel_ready = sem("sel_ready")
        h_in = sem("h_in")
        x_in = sem("x_nat_in")
        ht_ready = sem("ht_ready")
        hsq_ready = sem("hsq_ready")
        l_done = sem("logits_done")
        route = sem("route")
        norm_ready = sem("norm_ready")
        shifted_ready = sem("shifted_ready")
        exp_ready = sem("exp_ready")
        sumsq_ready = sem("sumsq_ready")
        comb_ready = sem("comb_ready")
        b_done = sem("broadcast_done")
        bcs_ready = sem("weight_ready")
        u_done = sem("hidden_done")
        us_ready = sem("scaled_ready")
        y_done = sem("y_done")
        yo_ready = sem("y_out_ready")
        y_out = [sem(f"y_out_dma{s}") for s in range(KY)]
        block = ctx.enter_context(nc.Block())
        ROUTE = 21
        NY = B * NH

        @block.sync
        def _(sp):
            def load(n):
                sp.dma_start(h_raw[:, :, :, :].rearrange("p t c b -> p t (c b)"),
                             hist_dram[:, bass.ds(n * TB, TB), :]).then_inc(h_in, DMA)

            for s in range(KY):
                sp.sem_inc(y_out[s], DMA * START)
            load(0)
            sp.wait_ge(rw_zero, 1)
            sp.dma_start(rw[:, :, 0:E], router_w.rearrange("(c p) e -> p c e", p=P),
                         allow_slow_non_contiguous=True).then_inc(rw_in, DMA)
            for e in range(E):
                sp.dma_start(wa[:, e, :, :], w_a[e, :, :].rearrange("(c p) r -> p c r", p=P)).then_inc(wa_in[e], DMA)
            for e in range(E):
                sp.dma_start(wb[:, e, :], w_b[e, :, :]).then_inc(wb_in, DMA)

            def outputs(n, last):
                if not last:
                    sp.wait_ge(ht_ready, B * (n + 1))
                    load(n + 1)
                sp.wait_ge(yo_ready, START + n * NY)
                sp.dma_start(x_nat[:, :, :], x[:, bass.ds(n * TB, TB), :].rearrange("b t d -> t b d"))\
                  .then_inc(x_in, DMA)
                for y in range(NY):
                    sp.wait_ge(yo_ready, START + n * NY + y + 1)
                    sp.dma_start(out[y // NH, bass.ds(n * TB, TB), (y % NH) * 512:(y % NH + 1) * 512],
                                 yo[y % KY][:, :]).then_inc(y_out[y % KY], DMA)

            with sp.Fori(0, NB - 1) as n:
                outputs(n, False)
            outputs(NB - 1, True)
            for s in range(KY):
                sp.wait_ge(y_out[s], DMA * (START + NB * NY // KY))

        @block.gpsimd
        def _(pool):
            pool.wait_ge(sel_zero, 2)
            for k in range(NQ * SPLIT):
                nc.gpsimd.affine_select(out=sel[:, :, :], in_=sel[:, :, :], compare_op=ALU.not_equal, fill=1.0,
                                        base=-(Q * (k // SPLIT) + E * (k % SPLIT)), pattern=[[-1, E], [0, P]],
                                        channel_multiplier=1).then_inc(sel_ready, 1)
                pool.wait_ge(sel_ready, k + 1)
            nc.gpsimd.affine_select(out=low[:, :, :], in_=low[:, :, :], compare_op=ALU.is_gt, fill=0.0,
                                    base=0, pattern=[[1, E], [-1, E]], channel_multiplier=0)\
              .then_inc(sel_ready, 1)
            with pool.Fori(0, NB) as n:
                pool.wait_ge(sumsq_ready, n + 1)
                nc.gpsimd.tensor_tensor(norm0[:, :], lt[:, :, E], half[:, :], ALU.pow).then_inc(norm_ready, 1)

        @block.scalar
        def _(act):
            act.sem_inc(bcs_ready, START)
            with act.Fori(0, NB) as n:
                act.wait_ge(h_in, DMA * (n + 1))
                act.wait_ge(u_done, START + n * E)
                for b in range(B):
                    nc.scalar.activation(ht[:, :, b, :], h_raw[:, :, :, b].rearrange("p t c -> p c t"),
                                         ACT.Copy).then_inc(ht_ready, 1)
                for b in range(B):
                    act.wait_ge(ht_ready, B * n + b + 1)
                    nc.scalar.activation(hsq[:, :, b, :], ht[:, :, b, :], ACT.Square).then_inc(hsq_ready, 1)
                act.wait_ge(shifted_ready, n + 1)
                nc.scalar.activation(expd[:, :, :], shifted[:, :, :], ACT.Exp).then_inc(exp_ready, 1)
                for e in range(E):
                    act.wait_ge(b_done, START + n * E + e + 1)
                    if e >= KB:
                        act.wait_ge(us_ready, START + n * E + e - KB + 1)
                    else:
                        act.wait_ge(us_ready, START + n * E)
                    nc.scalar.activation(bcs[e % KB][:, :], ps_b[e % KB][:, :], ACT.Copy).then_inc(bcs_ready, 1)

        @block.vector
        def _(dve):
            dve.sem_inc(us_ready, START)
            dve.sem_inc(yo_ready, START)
            nc.vector.memset(rw[:, :, :], 0.0).then_inc(rw_zero, 1)
            nc.vector.memset(sel[:, :, :], 0.0).then_inc(sel_zero, 1)
            nc.vector.memset(low[:, :, :], 1.0).then_inc(sel_zero, 1)
            nc.vector.memset(one_col[:, :], 0.0).then_inc(consts, 1)
            nc.vector.memset(half[:, :], 0.5).then_inc(consts, 1)
            nc.vector.memset(comb_parts[:, :, :], 0.0).then_inc(consts, 1)
            nc.vector.memset(comb_t[:, :, :], 0.0).then_inc(consts, 1)
            dve.wait_ge(consts, 4)
            nc.vector.memset(one_col[:, E:E + 1], 1.0).then_inc(consts, 1)
            dve.wait_ge(sel_ready, NQ * SPLIT + 1)

            def wide(a):
                return a.unsqueeze(2).broadcast_to([P, TK, E])

            with dve.Fori(0, NB) as n:
                at = [0]

                def link(ins):
                    at[0] += 1
                    ins.then_inc(route, 1)
                    dve.wait_ge(route, n * ROUTE + at[0])

                dve.wait_ge(l_done, n + 1)
                nc.vector.transpose(lt[:, :, :], ps_l[:, 0:P].rearrange("p (k i) -> p k i", i=Q))\
                  .then_inc(sumsq_ready, 1)
                dve.wait_ge(norm_ready, n + 1)
                link(nc.vector.tensor_scalar(norm[:, :], norm0[:, :], 1e-12, None, ALU.max))
                link(nc.vector.reciprocal(rnorm[:, :], norm[:, :]))
                link(nc.vector.tensor_tensor(logit[:, :, :], lt[:, :, 0:E], wide(rnorm[:, :]), ALU.mult))
                link(nc.vector.tensor_reduce(top[:, :], logit[:, :, :], AX.X, ALU.max))
                nc.vector.tensor_tensor(shifted[:, :, :], logit[:, :, :], wide(top[:, :]), ALU.subtract)\
                  .then_inc(shifted_ready, 1)
                dve.wait_ge(exp_ready, n + 1)
                link(nc.vector.tensor_reduce(total[:, :], expd[:, :, :], AX.X, ALU.add))
                link(nc.vector.reciprocal(rtotal[:, :], total[:, :]))
                link(nc.vector.tensor_tensor(prob[:, :, :], expd[:, :, :], wide(rtotal[:, :]), ALU.mult))
                pe_ = prob[:, :, :].unsqueeze(3).broadcast_to([P, TK, E, E])
                pf_ = prob[:, :, :].unsqueeze(2).broadcast_to([P, TK, E, E])
                link(nc.vector.tensor_tensor(above[:, :, :, :], pf_, pe_, ALU.is_gt))
                link(nc.vector.tensor_tensor(equal[:, :, :, :], pf_, pe_, ALU.is_equal))
                link(nc.vector.tensor_tensor(before[:, :, :, :], equal[:, :, :, :],
                                             low[:, :, :].unsqueeze(1).broadcast_to([P, TK, E, E]), ALU.mult))
                link(nc.vector.tensor_tensor(ahead[:, :, :, :], before[:, :, :, :], above[:, :, :, :], ALU.add))
                link(nc.vector.tensor_reduce(rank[:, :, :], ahead[:, :, :, :], AX.X, ALU.add))
                link(nc.vector.tensor_scalar(taken[:, :, :], rank[:, :, :], 2.0, None, ALU.is_lt))
                link(nc.vector.tensor_tensor(kept[:, :, :], taken[:, :, :], prob[:, :, :], ALU.mult))
                link(nc.vector.tensor_reduce(ksum[:, :], kept[:, :, :], AX.X, ALU.add))
                link(nc.vector.reciprocal(rksum[:, :], ksum[:, :]))
                link(nc.vector.tensor_tensor(comb[:, :, :], kept[:, :, :], wide(rksum[:, :]), ALU.mult))
                link(nc.vector.tensor_copy(comb_parts[:, :, 0:E], comb[:, :, :]))
                link(nc.vector.tensor_tensor(comb_rest[:, :, :], comb[:, :, :], comb_parts[:, :, 0:E], ALU.subtract))
                link(nc.vector.tensor_copy(comb_parts[:, :, E:2 * E], comb_rest[:, :, :]))
                link(nc.vector.tensor_tensor(comb_parts[:, :, 2 * E:3 * E], comb_rest[:, :, :],
                                             comb_parts[:, :, E:2 * E], ALU.subtract))
                dve.wait_ge(b_done, START + n * E)
                for j in range(NQ):
                    ins = nc.vector.transpose(
                        comb_t[j * Q:(j + 1) * Q, j, :].rearrange("p (k i) -> p k i", i=Q),
                        comb_parts[j * Q:(j + 1) * Q, :, :])
                ins.then_inc(comb_ready, 1)
                assert at[0] == ROUTE, at
                dve.wait_ge(y_done, START + n * NY)
                for e in range(E):
                    dve.wait_ge(u_done, START + n * E + e + 1)
                    dve.wait_ge(bcs_ready, START + n * E + e + 1)
                    nc.vector.tensor_tensor(us[:, e, :, :].rearrange("p b t -> p (b t)"), ps_u[e % KU][:, :],
                                            bcs[e % KB][:, :], ALU.mult).then_inc(us_ready, 1)
                dve.wait_ge(x_in, DMA * (n + 1))
                for y in range(NY):
                    dve.wait_ge(y_done, START + n * NY + y + 1)
                    dve.wait_ge(y_out[y % KY], DMA * (START + n * (NY // KY) + y // KY))
                    nc.vector.tensor_tensor(yo[y % KY][:, :], ps_y[y % KY][:, :],
                                            x_nat[:, y // NH, (y % NH) * 512:(y % NH + 1) * 512], ALU.add)\
                      .then_inc(yo_ready, 1)

        @block.tensor
        def _(pe):
            for s in (u_done, b_done, y_done):
                pe.sem_inc(s, START)
            pe.wait_ge(consts, 5)
            pe.wait_ge(rw_in, DMA)
            pe.wait_ge(sel_ready, NQ * SPLIT + 1)
            with pe.Fori(0, NB) as n:
                def hidden(e):
                    if e >= KU:
                        pe.wait_ge(us_ready, START + n * E + e - KU + 1)
                    else:
                        pe.wait_ge(us_ready, START + n * E)
                    pe.wait_ge(wa_in[e], DMA)
                    for c in range(NC):
                        ins = nc.tensor.matmul(ps_u[e % KU][:, :], wa[:, e, c, :],
                                               ht[:, c, :, :].rearrange("p b t -> p (b t)"),
                                               start=(c == 0), stop=(c == NC - 1))
                    ins.then_inc(u_done, 1)

                def broadcast(e):
                    if e >= KB:
                        pe.wait_ge(bcs_ready, START + n * E + e - KB + 1)
                    else:
                        pe.wait_ge(bcs_ready, START + n * E)
                    nc.tensor.matmul(ps_b[e % KB][:, :], sel[:, e, :],
                                     comb_t[:, :, :].rearrange("p b t -> p (b t)"),
                                     start=True, stop=True).then_inc(b_done, 1)

                pe.wait_ge(ht_ready, B * (n + 1))
                for c in range(NC):
                    for b in range(B):
                        nc.tensor.matmul(ps_l[b * Q:(b + 1) * Q, 0:TB], rw[:, c, :], ht[:, c, b, :],
                                         start=(c == 0), stop=False)
                pe.wait_ge(hsq_ready, B * (n + 1))
                for c in range(NC):
                    for b in range(B):
                        ins = nc.tensor.matmul(ps_l[b * Q:(b + 1) * Q, 0:TB], one_col[:, :], hsq[:, c, b, :],
                                               start=False, stop=(c == NC - 1))
                ins.then_inc(l_done, 1)
                hidden(0)
                hidden(1)
                pe.wait_ge(comb_ready, n + 1)
                broadcast(0)
                for e in range(2, E):
                    broadcast(e - 1)
                    hidden(e)
                broadcast(E - 1)
                pe.wait_ge(wb_in, DMA * E)
                for y in range(NY):
                    b, hf = y // NH, y % NH
                    for e in range(E):
                        pe.wait_ge(us_ready, START + n * E + e + 1)
                        if y < KY and e == 0:
                            pe.wait_ge(yo_ready, START + n * NY)
                        elif e == 0:
                            pe.wait_ge(yo_ready, START + n * NY + y - KY + 1)
                        ins = nc.tensor.matmul(ps_y[y % KY][:, :], us[:, e, b, :], wb[:, e, hf * 512:(hf + 1) * 512],
                                               start=(e == 0), stop=(e == E - 1))
                    ins.then_inc(y_done, 1)


def build(nc, x, h_start, w_ih, w_hh, b_ih, b_hh, router_w, w_a, w_b, out):
    B, T, D = x.shape
    gi_dram = nc.dram_tensor("gi_scratch", [P, T, GATES * D // P * B], FP32, kind="Internal").ap()
    hist_dram = nc.dram_tensor("h_scratch", [P, T, D // P * B], FP32, kind="Internal").ap()
    input_projection(nc, x, w_ih, b_ih, b_hh, gi_dram)
    recurrence(nc, h_start, w_hh, b_hh, gi_dram, hist_dram)
    routed_ffn(nc, x, hist_dram, router_w, w_a, w_b, out)


_INS = ['x', 'cond_2048', 'L0_cond_W_ih', 'L0_cond_W_hh', 'L0_cond_b_ih', 'L0_cond_b_hh',
        'L0_ffn_router_w', 'L0_ffn_Wa', 'L0_ffn_Wb']


def kernel(**inputs):
    import numpy as _np
    import concourse.bacc as _bacc
    from concourse import mybir as _mybir
    from concourse.bass_utils import run_bass_kernel_spmd as _run

    nc = _bacc.Bacc("TRN2", target_bir_lowering=False, num_devices=1)
    arrays, args = {}, []
    for name in _INS:
        a = _np.ascontiguousarray(inputs[name])
        arrays[f"in_{name}"] = a
        args.append(nc.dram_tensor(f"in_{name}", a.shape, _mybir.dt.from_np(a.dtype), kind="ExternalInput").ap())
    shape = inputs['x'].shape
    args.append(nc.dram_tensor("out", shape, _mybir.dt.float32, kind="ExternalOutput").ap())
    build(nc, *args)
    r = _run(nc, [arrays], core_ids=[0])
    return r.results[0]["out"]
```
